# Optimizing a Trainium2 kernel written in Bass

```python
import numpy as np
import jax
import jax.numpy as jnp

def _softmax(x, axis=-1):
    return jax.nn.softmax(x, axis=axis)

def _gelu(x):
    return jax.nn.gelu(x, approximate=True)

def _silu(x):
    return jax.nn.silu(x)

def _sigmoid(x):
    return jax.nn.sigmoid(x)

def _layernorm(x, axis=-1, eps=1e-05):
    m = jnp.mean(x, axis=axis, keepdims=True)
    v = jnp.var(x, axis=axis, keepdims=True)
    return (x - m) / jnp.sqrt(v + eps)

def _scatter_add(tgt, idx, src, axis=0):
    return tgt.at[idx].add(src)

def _segment_sum(src, seg, n):
    return jax.ops.segment_sum(src, seg, n)
kernel_name = 'mk_cond_resid_d4_seqx_r8_35803b'

def setup_inputs(seed: int=0):
    np.random.seed(seed)
    _w = jnp.asarray

    def _rec_inputs():
        import jax
        import jax.numpy as jnp
        _rk = jax.random.key(seed)
        x = -0.000125 + 0.9999 * jax.random.normal(jax.random.fold_in(_rk, 1), (32, 32, 256), jnp.float32)
        _lenS = 32 - jax.random.randint(jax.random.fold_in(_rk, 7), (32,), 0, max(1, 32 // 4) + 1, jnp.int32)
        _lenS2 = 32 - jax.random.randint(jax.random.fold_in(_rk, 8), (32,), 0, max(1, 32 // 4) + 1, jnp.int32)
        itok_B_0_7 = jax.random.randint(jax.random.fold_in(_rk, 11), (32,), 0, 8, jnp.int32)
        fside_8xS_0 = -0.00162727 + 0.0609077 * jax.random.normal(jax.random.fold_in(_rk, 12), (8, 32), jnp.float32)
        itok_B_0_3 = jax.random.randint(jax.random.fold_in(_rk, 13), (32,), 0, 4, jnp.int32)
        itok_B_1_198 = jax.random.randint(jax.random.fold_in(_rk, 14), (32,), 1, 199, jnp.int32)
        return (x, itok_B_0_7, fside_8xS_0, itok_B_0_3, itok_B_1_198)
    x, itok_B_0_7, fside_8xS_0, itok_B_0_3, itok_B_1_198 = _rec_inputs()

    def _L0_cond_setup():
        import jax, jax.numpy as jnp
        import numpy as np
        B, C, T = (64, 32, 256)
        D, N = (32, 8)
        key = jax.random.key(seed)
        k_x, k_s, k_w, k_b = jax.random.split(key, 4)
        scale = 1.0 / np.sqrt(C)
        x = jax.random.normal(k_x, (B, C, T), dtype=jnp.float32)
        subjects = jax.random.randint(k_s, (B,), 0, N, dtype=jnp.int64)
        weights = jax.random.normal(k_w, (N, C, D), dtype=jnp.float32) * scale
        bias = jax.random.normal(k_b, (N, D), dtype=jnp.float32) * scale
        return {'x': x, 'subjects': subjects, 'weights': weights, 'bias': bias}
    _L0_cond_all = _L0_cond_setup()
    _L0_cond_in = {k: v for k, v in _L0_cond_all.items() if k in ('weights',)}
    del _L0_cond_all

    def _L1_cond_setup():
        import jax, jax.numpy as jnp
        import numpy as np
        B, C, D, T, N_SUBJECTS = (128, 32, 32, 256, 8)
        key = jax.random.key(seed)
        kx, ks, kw = jax.random.split(key, 3)
        x = jax.random.normal(kx, (B, C, T), dtype=jnp.float32)
        subjects = jax.random.randint(ks, (B,), 0, N_SUBJECTS, dtype=jnp.int64)
        weights = jax.random.normal(kw, (N_SUBJECTS, C, D), dtype=jnp.float32) * (1.0 / C ** 0.5)
        return {'x': x, 'subjects': subjects, 'weights': weights}
    _L1_cond_all = _L1_cond_setup()
    _L1_cond_in = {k: v for k, v in _L1_cond_all.items() if k in ('weights',)}
    del _L1_cond_all

    def _L2_cond_setup():
        import jax, jax.numpy as jnp
        import numpy as np
        B, S, D_IN, D_OUT, R, E = (8, 256, 256, 256, 16, 4)
        key = jax.random.key(seed)
        ks = jax.random.split(key, 7)
        x = jax.random.normal(ks[0], (B, S, D_IN), dtype=jnp.float32)
        W_base = jax.random.normal(ks[1], (D_OUT, D_IN), dtype=jnp.float32) * 0.02
        Wt = jax.random.normal(ks[2], (D_IN, D_IN), dtype=jnp.float32) * 0.02
        A = jax.random.normal(ks[3], (E, R, D_IN), dtype=jnp.float32) * 0.02
        B_w = jax.random.normal(ks[4], (E, D_OUT, R), dtype=jnp.float32) * 0.02
        Wp = jax.random.normal(ks[5], (D_OUT, D_OUT), dtype=jnp.float32) * 0.02
        scaling = jnp.ones((E,), dtype=jnp.float32)
        adapter_idx = jax.random.randint(ks[6], (B,), 0, E)
        return {'x': x, 'W_base': W_base, 'Wt': Wt, 'A': A, 'B_w': B_w, 'Wp': Wp, 'scaling': scaling, 'adapter_idx': adapter_idx}
    _L2_cond_all = _L2_cond_setup()
    _L2_cond_in = {k: v for k, v in _L2_cond_all.items() if k in ('W_base', 'Wt', 'A', 'B_w', 'Wp', 'scaling')}
    del _L2_cond_all

    def _L3_cond_setup():
        import jax, jax.numpy as jnp
        import numpy as np
        B, C, T = (128, 32, 256)
        S, D = (200, 32)
        key = jax.random.key(seed)
        k1, k2, k3 = jax.random.split(key, 3)
        x = jax.random.normal(k1, (B, C, T), dtype=jnp.float32)
        conditions = jax.random.randint(k2, (B,), 0, S, dtype=jnp.int64)
        weights = jax.random.normal(k3, (S, C, D), dtype=jnp.float32) / jnp.sqrt(jnp.float32(C))
        return {'x': x, 'conditions': conditions, 'weights': weights}
    _L3_cond_all = _L3_cond_setup()
    _L3_cond_in = {k: v for k, v in _L3_cond_all.items() if k in ('weights',)}
    del _L3_cond_all
    return {'x': x, 'itok_B_0_7': itok_B_0_7, 'fside_8xS_0': fside_8xS_0, 'itok_B_0_3': itok_B_0_3, 'itok_B_1_198': itok_B_1_198, 'L0_cond_weights': _L0_cond_in['weights'], 'L1_cond_weights': _L1_cond_in['weights'], 'L2_cond_W_base': _L2_cond_in['W_base'], 'L2_cond_Wt': _L2_cond_in['Wt'], 'L2_cond_A': _L2_cond_in['A'], 'L2_cond_B_w': _L2_cond_in['B_w'], 'L2_cond_Wp': _L2_cond_in['Wp'], 'L2_cond_scaling': _L2_cond_in['scaling'], 'L3_cond_weights': _L3_cond_in['weights']}

def reference(x, itok_B_0_7, fside_8xS_0, itok_B_0_3, itok_B_1_198, L0_cond_weights, L1_cond_weights, L2_cond_W_base, L2_cond_Wt, L2_cond_A, L2_cond_B_w, L2_cond_Wp, L2_cond_scaling, L3_cond_weights):
    import jax
    import jax.numpy as jnp

    def _L0_cond_ref(x, subjects, weights, bias):
        import jax, jax.numpy as jnp
        import numpy as np
        B, C, T = (64, 32, 256)
        D, N = (32, 8)
        w = weights[subjects]
        b = bias[subjects]
        out = jnp.einsum('bct,bcd->bdt', x, w)
        out = out + b[:, :, None]
        return out

    def _L1_cond_ref(x, subjects, weights):
        import jax, jax.numpy as jnp
        import numpy as np
        B, C, D, T, N_SUBJECTS = (128, 32, 32, 256, 8)
        w = weights[subjects]
        out = jnp.einsum('bct,bcd->bdt', x, w)
        return out

    def _L2_cond_ref(x, W_base, Wt, A, B_w, Wp, scaling, adapter_idx):
        import jax, jax.numpy as jnp
        import numpy as np
        B, S, D_IN, D_OUT, R, E = (8, 256, 256, 256, 16, 4)
        base = jnp.einsum('bsi,oi->bso', x, W_base)
        h = jnp.einsum('bsi,ji->bsj', x, Wt)
        Ab = A[adapter_idx]
        Bb = B_w[adapter_idx]
        sc = scaling[adapter_idx]
        z = jnp.einsum('bsj,brj->bsr', h, Ab)
        l = jnp.einsum('bsr,bor->bso', z, Bb)
        lora_out = jnp.einsum('bso,po->bsp', l, Wp) * sc[:, None, None]
        return base + lora_out

    def _L3_cond_ref(x, conditions, weights):
        import jax, jax.numpy as jnp
        import numpy as np
        B, C, T = (128, 32, 256)
        S, D = (200, 32)
        w = weights[conditions]
        return jnp.einsum('bct,bcd->bdt', x, w)
    x = x + _L0_cond_ref(x, itok_B_0_7, L0_cond_weights, fside_8xS_0)
    x = x + _L1_cond_ref(x, itok_B_0_7, L1_cond_weights)
    x = x + _L2_cond_ref(x, L2_cond_W_base, L2_cond_Wt, L2_cond_A, L2_cond_B_w, L2_cond_Wp, L2_cond_scaling, itok_B_0_3)
    x = x + _L3_cond_ref(x, itok_B_1_198, L3_cond_weights)
    return x

_drawn_inputs = setup_inputs


def setup_inputs(seed=0):
    import zlib

    import numpy as np

    out = dict(_drawn_inputs(seed))
    spreads = {'L2_cond_scaling': (1.0, 0.6)}
    factors = {'L2_cond_Wt': 8.0, 'L2_cond_A': 8.0, 'L2_cond_B_w': 8.0, 'L2_cond_Wp': 8.0}
    for name, (base, spread) in spreads.items():
        noise = np.random.default_rng([zlib.crc32(name.encode()), seed]).standard_normal(out[name].shape)
        drawn = base * np.exp(spread * noise) if base else spread * noise
        out[name] = jnp.asarray(drawn.astype(out[name].dtype))
    for name, factor in factors.items():
        out[name] = (out[name] * factor).astype(out[name].dtype)
    return out
```

```python
import concourse.bass as bass
from concourse import mybir
from contextlib import ExitStack

B, C, T = 32, 32, 256
SUBJECTS, CONDITIONS = 8, 200
EXPERTS, RANK = 4, 16
P = 128
J = P // C
G = B // J
KC = T // P
ER = EXPERTS * RANK
R4 = P // B
C8 = C // R4
SROWS = SUBJECTS * R4
QW = C + R4
SW = 2 * C8 * C + C


def cond_resid(nc, idx_col, idx_row, subj, const, ab, wtp, x, wb, w3, out):
    fp32, i32 = mybir.dt.float32, mybir.dt.int32
    ALU = mybir.AluOpType

    with ExitStack() as ctx:
        def sb(name, shape, dt=fp32):
            return ctx.enter_context(nc.sbuf_tensor(name, shape, dt))

        def sem(name):
            return ctx.enter_context(nc.semaphore(name))

        cond_col = sb("cond_col", [P, 2], i32)
        cond_rows = sb("cond_rows", [P, 1], i32)
        rows_sb = sb("rows_sb", [P, 2 * B], i32)
        subj_sb = sb("subj_sb", [SROWS + R4, SW + P])
        const_sb = sb("const_sb", [P, 3 + C + P])
        ab_sb = sb("ab_sb", [P, KC, 2, ER])
        wtp_sb = sb("wtp_sb", [P, 2, KC, T])
        x_sb = sb("x_sb", [P, G, T])
        m_sb = sb("m_sb", [P, KC, T])
        subject_of, expert_of, scale_of = (const_sb[:, i:i + 1] for i in range(3))
        eye_c = const_sb[:, 3:3 + C]
        eye_p = const_sb[:, 3 + C:3 + C + P]
        table = subj_sb[:, 0:SW]
        onehot = subj_sb[:, SW:SW + P]

        w3_rows = sb("w3_rows", [P, C8 * C])
        l3raw = sb("l3raw", [P, G, C])
        l3 = sb("l3", [P, G, C])
        l10 = sb("l10", [P, G, SW // C * R4])
        qt = sb("qt", [P, G, QW])
        bd = sb("bd", [P, G, P])
        ql3 = sb("ql3", [P, G, C])
        ones = sb("ones", [P, P])
        cb = sb("cb", [P, G, J, C])
        x2t = sb("x2t", [P, G, KC, P])
        gt = sb("gt", [P, KC, ER])
        h = sb("h", [ER, T])
        mask = sb("mask", [ER, B])
        z = sb("z", [ER, G * P])
        y = sb("y", [P, G, T])

        bank = [ctx.enter_context(nc.psum_tensor(f"bank{i}", [P, 512], fp32)) for i in range(8)]
        sel_ps = bank[0][:, 0:2 * C8 * C]
        selb_ps = bank[1][:, 0:C]
        qt_ps = bank[1][:, C:C + G * QW].rearrange("p (g c) -> p g c", g=G)
        gt_ps = bank[2][:, 0:KC * ER].rearrange("p (k n) -> p k n", k=KC)
        h_ps = bank[2][0:ER, T:2 * T]
        p_ps = bank[3][:, 0:G * C].rearrange("p (g d) -> p g d", g=G)
        c_ps = [bank[4 + j][:, 0:G * C] for j in range(J)]
        a_ps = [bank[0], bank[1], bank[2], bank[3]]
        z_ps = [bank[4], bank[5]]
        y_ps = [bank[6], bank[7], bank[0], bank[1], bank[2], bank[3]]

        cond_loaded, rows_loaded, subj_loaded, const_loaded = map(sem, ("cond_l", "rows_l", "subj_l", "const_l"))
        ab_loaded, wt_loaded, wp_loaded, wb_loaded, w3_loaded = map(sem, ("ab_l", "wt_l", "wp_l", "wb_l", "w3_l"))
        x_loaded = [sem(f"x_l{i}") for i in range(2)]
        stored = sem("stored")
        ones_done, bd_cleared, cond_rows_done = sem("ones_done"), sem("bd_cleared"), sem("cond_rows_done")
        onehot_done, sel_done, l10_done = sem("onehot_done"), sem("sel_done"), sem("l10_done")
        qt_mm, qt_done, l3raw_done, l3_done = sem("qt_mm"), sem("qt_done"), sem("l3raw_done"), sem("l3_done")
        p_mm, bd_act, bd_dve, ql3_done = sem("p_mm"), sem("bd_act"), sem("bd_dve"), sem("ql3_done")
        c_mm, c_done = sem("c_mm"), sem("c_done")
        gh_mm, gh_done, m_done, mask_done = sem("gh_mm"), sem("gh_done"), sem("m_done"), sem("mask_done")
        a_mm, x2t_done, z_mm, z_done = sem("a_mm"), sem("x2t_done"), sem("z_mm"), sem("z_done")
        y_mm, y_act, y_dve = sem("y_mm"), sem("y_act"), sem("y_dve")

        block = ctx.enter_context(nc.Block())
        HALF = G // 2

        @block.sync
        def _(sp):
            sp.dma_start(cond_col[:, :], idx_col).then_inc(cond_loaded, 16)
            sp.dma_start(rows_sb[:, :], idx_row.partition_broadcast(P)).then_inc(rows_loaded, 16)
            sp.dma_start(const_sb[:, :], const).then_inc(const_loaded, 16)
            sp.dma_start(wtp_sb[:, 0], wtp[:, 0]).then_inc(wt_loaded, 16)
            sp.dma_start(x_sb[:, 0:HALF], x[:, 0:HALF]).then_inc(x_loaded[0], 16)
            sp.dma_start(x_sb[:, HALF:G], x[:, HALF:G]).then_inc(x_loaded[1], 16)
            for n in range(G // 2):
                sp.wait_ge(y_act, n + 1)
                sp.wait_ge(y_dve, n + 1)
                sp.dma_start(out[:, 2 * n:2 * n + 2], y[:, 2 * n:2 * n + 2]).then_inc(stored, 16)
            sp.wait_ge(stored, 16 * (G // 2))

        @block.gpsimd
        def _(pool):
            nc.gpsimd.memset(ones[:, :], 1.0).then_inc(ones_done, 1)
            nc.gpsimd.memset(bd[:, :, :], 0.0).then_inc(bd_cleared, 1)
            pool.wait_ge(cond_loaded, 16)
            nc.gpsimd.tensor_scalar(cond_rows[:, :], cond_col[:, 0:1], float(R4), cond_col[:, 1:2],
                                    ALU.mult, ALU.add).then_inc(cond_rows_done, 1)
            pool.wait_ge(cond_rows_done, 1)
            pool.indirect_dma_start(w3_rows[:, :], None, w3,
                                    bass.IndirectOffsetOnAxis(ap=cond_rows[:, :], axis=0)).then_inc(w3_loaded, 16)
            pool.wait_ge(wb_loaded, 16)
            pool.wait_ge(const_loaded, 16)
            for k in range(KC):
                diag = m_sb[:, k, k * P:(k + 1) * P]
                nc.gpsimd.tensor_tensor(diag, diag, eye_p, ALU.add).then_inc(m_done, 1)

        @block.scalar
        def _(act):
            act.dma_start(subj_sb[:, :], subj).then_inc(subj_loaded, 16)
            act.dma_start(ab_sb[:, :, :, :], ab).then_inc(ab_loaded, 16)
            act.dma_start(wtp_sb[:, 1], wtp[:, 1]).then_inc(wp_loaded, 16)
            act.dma_start(m_sb[:, :, :], wb).then_inc(wb_loaded, 16)
            act.wait_ge(qt_mm, 1)
            nc.scalar.copy(qt[:, :, :], qt_ps).then_inc(qt_done, 1)
            act.wait_ge(gh_mm, 1)
            nc.scalar.copy(gt[:, :, :], gt_ps)
            nc.scalar.copy(h[:, :], h_ps).then_inc(gh_done, 1)
            act.wait_ge(p_mm, 1)
            act.wait_ge(bd_cleared, 1)
            for j in range(J // 2, J):
                q = slice(C * j, C * j + C)
                last = nc.scalar.copy(bd[q, :, q], p_ps[q])
            last.then_inc(bd_act, 1)
            for j in range(J):
                act.wait_ge(c_mm, j + 1)
                nc.scalar.copy(cb[:, :, j, :], c_ps[j].rearrange("p (g d) -> p g d", g=G)).then_inc(c_done, 1)
            for g in range(0, G, 2):
                act.wait_ge(y_mm, g + 1)
                nc.scalar.copy(y[:, g, :], y_ps[g % len(y_ps)][:, 0:T]).then_inc(y_act, 1)

        @block.vector
        def _(dve):
            dve.wait_ge(rows_loaded, 16)
            dve.wait_ge(subj_loaded, 16)
            dve.wait_ge(const_loaded, 16)
            pattern = onehot[0:SROWS, :].rearrange("p (b r) -> p b r", r=R4)
            nc.vector.scalar_tensor_tensor(
                out=pattern, in0=rows_sb[0:SROWS, 0:B].unsqueeze(2).broadcast_to([SROWS, B, R4]),
                scalar=subject_of[0:SROWS, :], in1=pattern, op0=ALU.is_equal, op1=ALU.mult).then_inc(onehot_done, 1)
            nc.vector.tensor_scalar(mask[:, :], rows_sb[0:ER, B:2 * B], expert_of[0:ER, :], scale_of[0:ER, :],
                                    ALU.is_equal, ALU.mult).then_inc(mask_done, 1)
            dve.wait_ge(sel_done, 1)
            blocks = l10[:, :, :].rearrange("p g (a b) -> p a g b", b=R4)
            nc.vector.transpose(blocks[:, 0:2 * C8], sel_ps.rearrange("p (a g b) -> p a g b", g=G, b=R4))
            nc.vector.transpose(blocks[:, 2 * C8:], selb_ps.rearrange("p (a g b) -> p a g b", g=G, b=R4)).then_inc(l10_done, 1)
            dve.wait_ge(w3_loaded, 16)
            nc.vector.transpose(l3raw[:, :, :].rearrange("p g (a b) -> p a g b", b=R4),
                                w3_rows[:, :].rearrange("p (a g b) -> p a g b", g=G, b=R4)).then_inc(l3raw_done, 1)
            dve.wait_ge(l3raw_done, 1)
            nc.vector.tensor_tensor(l3[:, :, :], l3raw[:, :, :], eye_c.unsqueeze(1).broadcast_to([P, G, C]),
                                    ALU.add).then_inc(l3_done, 1)
            dve.wait_ge(l3_done, 1)
            dve.wait_ge(qt_done, 1)
            nc.vector.tensor_tensor(ql3[:, :, :], l3[:, :, :], qt[:, :, C:C + 1].broadcast_to([P, G, C]),
                                    ALU.mult).then_inc(ql3_done, 1)
            dve.wait_ge(p_mm, 1)
            dve.wait_ge(bd_cleared, 1)
            for j in range(J // 2):
                q = slice(C * j, C * j + C)
                last = nc.vector.tensor_copy(bd[q, :, q], p_ps[q])
            last.then_inc(bd_dve, 1)
            dve.wait_ge(c_done, J)
            for n in range(G // 2):
                dve.wait_ge(a_mm, n + 1)
                pair = slice(2 * n, 2 * n + 2)
                bias = cb[:, pair].rearrange("p g j d -> p g (j d)").unsqueeze(2).broadcast_to([P, 2, KC, P])
                nc.vector.tensor_tensor(x2t[:, pair], a_ps[n][:, :].rearrange("p (g k n) -> p g k n", g=2, k=KC),
                                        bias, ALU.add).then_inc(x2t_done, 1)
            for n in range(2):
                dve.wait_ge(z_mm, n + 1)
                dve.wait_ge(mask_done, 1)
                half = slice(HALF * P * n, HALF * P * (n + 1))
                nc.vector.tensor_tensor(
                    z[:, half].rearrange("p (b d) -> p b d", d=C),
                    z_ps[n][0:ER, :].rearrange("p (b d) -> p b d", d=C),
                    mask[:, B // 2 * n:B // 2 * (n + 1)].unsqueeze(2).broadcast_to([ER, B // 2, C]),
                    ALU.mult).then_inc(z_done, 1)
            for g in range(1, G, 2):
                dve.wait_ge(y_mm, g + 1)
                nc.vector.tensor_copy(y[:, g, :], y_ps[g % len(y_ps)][:, 0:T]).then_inc(y_dve, 1)

        @block.tensor
        def _(pe):
            mm = nc.tensor.matmul
            pe.wait_ge(onehot_done, 1)
            mm(sel_ps, onehot, table[:, 0:2 * C8 * C], start=True, stop=True)
            mm(selb_ps, onehot, table[:, 2 * C8 * C:SW], start=True, stop=True).then_inc(sel_done, 1)
            pe.wait_ge(l10_done, 1)
            for g in range(G):
                for j in range(J):
                    q = slice(C * j, C * j + C)
                    last = mm(qt_ps[q, g, :], l10[q, g, 0:C], l10[q, g, C:C + QW],
                              start=True, stop=True, tile_position=(C * j, C * j))
            last.then_inc(qt_mm, 1)
            pe.wait_ge(ab_loaded, 16)
            pe.wait_ge(wt_loaded, 16)
            for k in range(KC):
                for c in range(KC):
                    mm(gt_ps[:, k, :], wtp_sb[:, 0, c, k * P:(k + 1) * P], ab_sb[:, c, 0, :],
                       start=(c == 0), stop=(c == KC - 1))
            pe.wait_ge(wp_loaded, 16)
            for c in range(KC):
                last = mm(h_ps, ab_sb[:, c, 1, :], wtp_sb[:, 1, c, :], start=(c == 0), stop=(c == KC - 1))
            last.then_inc(gh_mm, 1)
            pe.wait_ge(qt_done, 1)
            pe.wait_ge(l3_done, 1)
            for g in range(G):
                for j in range(J):
                    q = slice(C * j, C * j + C)
                    last = mm(p_ps[q, g, :], qt[q, g, 0:C], l3[q, g, :], start=True, stop=True,
                              tile_position=(C * j, C * j))
            last.then_inc(p_mm, 1)
            pe.wait_ge(ones_done, 1)
            pe.wait_ge(ql3_done, 1)
            for j in range(J):
                q = slice(C * j, C * j + C)
                mm(c_ps[j], ones[q, :], ql3[q, :, :], start=True, stop=True,
                   tile_position=(C * j, 0)).then_inc(c_mm, 1)
            pe.wait_ge(bd_act, 1)
            pe.wait_ge(bd_dve, 1)
            pe.wait_ge(gh_done, 1)
            for n in range(G // 2):
                if n % 2 == 0:
                    pe.wait_ge(x_loaded[n // 2], 16)
                for g in range(2 * n, 2 * n + 2):
                    for k in range(KC):
                        at = ((g % 2) * KC + k) * P
                        last = mm(a_ps[n][:, at:at + P], x_sb[:, g, k * P:(k + 1) * P], bd[:, g, :],
                                  start=True, stop=True)
                last.then_inc(a_mm, 1)
            pe.wait_ge(c_done, J)
            for n in range(2):
                pe.wait_ge(x2t_done, G // 4 * (n + 1))
                for k in range(KC):
                    last = mm(z_ps[n][0:ER, :], gt[:, k, :], x2t[:, HALF * n:HALF * (n + 1), k, :],
                              start=(k == 0), stop=(k == KC - 1))
                last.then_inc(z_mm, 1)
            pe.wait_ge(m_done, KC)
            for g in range(G):
                if g >= len(y_ps):
                    pe.wait_ge(y_dve if g % 2 else y_act, (g - len(y_ps)) // 2 + 1)
                acc = y_ps[g % len(y_ps)][:, 0:T]
                for k in range(KC):
                    mm(acc, x2t[:, g, k, :], m_sb[:, k, :], start=(k == 0), stop=False)
                if g % HALF == 0:
                    pe.wait_ge(z_done, g // HALF + 1)
                mm(acc, z[:, P * g:P * (g + 1)], h[:, :], start=False, stop=True).then_inc(y_mm, 1)


def kernel(**inputs):
    import numpy as _np
    import concourse.bacc as _bacc
    from concourse import mybir as _mybir
    from concourse.bass_utils import run_bass_kernel_spmd as _run

    a = {k: _np.asarray(v) for k, v in inputs.items()}
    f32 = a["x"].dtype

    w0 = a["L0_cond_weights"].reshape(SUBJECTS, C8, R4, C).transpose(0, 2, 1, 3).reshape(SROWS, C8 * C)
    w1 = a["L1_cond_weights"].reshape(SUBJECTS, C, C8, R4).transpose(0, 3, 2, 1).reshape(SROWS, C8 * C)
    bias = _np.repeat(a["fside_8xS_0"], R4, axis=0)
    eye = _np.eye(C, dtype=f32).reshape(C8, R4, C).transpose(1, 0, 2).reshape(R4, C8 * C)
    table = _np.concatenate([_np.concatenate([w1, w0, bias], 1),
                             _np.concatenate([eye, eye, _np.zeros((R4, C), f32)], 1)], 0)
    pattern = _np.tile(_np.eye(R4, dtype=f32), (SUBJECTS + 1, B))
    part = _np.arange(P)
    scale = _np.tile(_np.repeat(a["L2_cond_scaling"], RANK), P // ER)[:, None]
    const = _np.concatenate([(part // R4)[:, None].astype(f32), (part % ER // RANK)[:, None].astype(f32), scale,
                             _np.tile(_np.eye(C, dtype=f32), (J, 1)), _np.eye(P, dtype=f32)], 1)

    def by_partition(m):
        return m.reshape(KC, P, -1).transpose(1, 0, 2)

    def jg(idx):
        return idx.reshape(G, J).T.reshape(B)

    cond = jg(a["itok_B_1_198"])
    arrays = {
        "idx_col": _np.stack([_np.repeat(cond, R4), (part % R4).astype(cond.dtype)], 1),
        "idx_row": _np.concatenate([jg(a["itok_B_0_7"]), a["itok_B_0_3"]]),
        "subj": _np.concatenate([table, pattern], 1),
        "const": const,
        "ab": _np.stack([by_partition(a["L2_cond_A"].reshape(ER, T).T),
                         by_partition(a["L2_cond_B_w"].transpose(1, 0, 2).reshape(T, ER))], 2),
        "wtp": _np.stack([by_partition(a["L2_cond_Wt"]), by_partition(a["L2_cond_Wp"].T)], 1),
        "x": a["x"].reshape(G, J, C, T).transpose(1, 2, 0, 3).reshape(P, G, T),
        "wb": by_partition(a["L2_cond_W_base"].T),
        "w3": a["L3_cond_weights"].transpose(0, 2, 1).reshape(CONDITIONS, C8, R4, C)
              .transpose(0, 2, 1, 3).reshape(CONDITIONS * R4, C8 * C),
    }
    arrays = {f"in_{k}": _np.ascontiguousarray(v) for k, v in arrays.items()}
    nc = _bacc.Bacc("TRN2", target_bir_lowering=False, num_devices=1)
    args = [nc.dram_tensor(k, v.shape, _mybir.dt.from_np(v.dtype), kind="ExternalInput").ap()
            for k, v in arrays.items()]
    out = nc.dram_tensor("out_y", (P, G, T), _mybir.dt.from_np(f32), kind="ExternalOutput").ap()
    cond_resid(nc, *args, out)
    r = _run(nc, [arrays], core_ids=[0])
    y = r.results[0]["out_y"]
    return y.reshape(J, C, G, T).transpose(2, 0, 1, 3).reshape(B, C, T)
```

```python
import concourse.bass as bass
from concourse import mybir
from contextlib import ExitStack

B, C, T = 32, 32, 256
SUBJECTS, CONDITIONS = 8, 200
EXPERTS, RANK = 4, 16
P = 128
J = P // C
G = B // J
KC = T // P
ER = EXPERTS * RANK
R4 = P // B
C8 = C // R4
SROWS = SUBJECTS * R4
QW = C + R4
SW = 2 * C8 * C + C


HALF = G // 2
CW = 2 + C + P + KC * 2 * ER
SPAD = 2 * SROWS
WARM = (7, 0, 1, 0)


def cond_resid(nc, idx_col, idx_row, subj, const, wtp, x, wb, w3, out):
    fp32, fp32r, bf16, i32 = mybir.dt.float32, mybir.dt.float32r, mybir.dt.bfloat16, mybir.dt.int32
    ALU = mybir.AluOpType

    with ExitStack() as ctx:
        def sb(name, shape, dt=fp32):
            return ctx.enter_context(nc.sbuf_tensor(name, shape, dt))

        def sem(name):
            return ctx.enter_context(nc.semaphore(name))

        cond_col = sb("cond_col", [P, 2], i32)
        cond_rows = sb("cond_rows", [P, 1], i32)
        rows_sb = sb("rows_sb", [P, 2 * B], i32)
        subj_sb = sb("subj_sb", [P, SW + P + 1])
        const_sb = sb("const_sb", [P, CW])
        wtp_sb = sb("wtp_sb", [P, 2, KC, T])
        x_sb = sb("x_sb", [P, G, T])
        m_sb = sb("m_sb", [P, KC, T])
        table = subj_sb[:, 0:SW]
        onehot = subj_sb[:, SW:SW + P]
        subject_of = subj_sb[:, SW + P:SW + P + 1]
        expert_of, scale_of = const_sb[:, 0:1], const_sb[:, 1:2]
        eye_c = const_sb[:, 2:2 + C]
        eye_p = const_sb[:, 2 + C:2 + C + P]
        ab_sb = const_sb[:, 2 + C + P:CW].rearrange("p (c w n) -> p c w n", c=KC, w=2)

        w3_rows = sb("w3_rows", [P, C8 * C])
        l3raw = sb("l3raw", [P, G, C])
        l3 = sb("l3", [P, G, C])
        l10 = sb("l10", [P, G, SW // C * R4])
        qt = sb("qt", [P, G, QW])
        bd = sb("bd", [P, G, P])
        ql3 = sb("ql3", [P, G, C])
        ql3_hi = sb("ql3_hi", [P, G, C], fp32r)
        ql3_lo = sb("ql3_lo", [P, G, C], fp32r)
        ones = sb("ones", [P, P])
        ones_r = sb("ones_r", [P, P], fp32r)
        cb = sb("cb", [P, G, J, C])
        x2t = sb("x2t", [P, G, KC, P])
        x2t_hi = sb("x2t_hi", [P, G, KC, P], fp32r)
        x2t_lo = sb("x2t_lo", [P, G, KC, P], fp32r)
        m_hi = sb("m_hi", [P, KC, T], fp32r)
        m_lo = sb("m_lo", [P, KC, T], fp32r)
        gt = sb("gt", [P, KC, ER])
        h = sb("h", [P, T])
        h_hi = sb("h_hi", [P, T], fp32r)
        h_lo = sb("h_lo", [P, T], fp32r)
        mask = sb("mask", [P, B // 2])
        z = sb("z", [P, HALF * P])
        z_hi = sb("z_hi", [P, HALF * P], fp32r)
        z_lo = sb("z_lo", [P, HALF * P], fp32r)
        y = sb("y", [P, G, T])
        warm = sb("warm", [P, P], bf16)

        bank = [ctx.enter_context(nc.psum_tensor(f"bank{i}", [P, 512], fp32)) for i in range(8)]
        sel_ps = [bank[0][:, 0:C8 * C], bank[1][:, 0:SW - C8 * C]]
        qt_ps = [bank[n][:, 320:320 + HALF * QW].rearrange("p (g c) -> p g c", g=HALF) for n in (1, 2)]
        p_ps = [bank[n][:, 0:HALF * C].rearrange("p (g d) -> p g d", g=HALF) for n in (3, 0)]
        a_ps = [bank[i] for i in (6, 7, 0, 3)]
        c_ps = [bank[i][:, 0:G * C] for i in (1, 2, 4, 5)]
        gt_ps = bank[4][:, 0:KC * ER].rearrange("p (k n) -> p k n", k=KC)
        h_ps = bank[5][:, 0:T]
        z_ps = bank[4]
        y_ps = [bank[i] for i in (5, 2, 1, 6, 7, 0, 3)]
        warm_ps = bank[7]

        cond_loaded, rows_loaded, subj_loaded, const_loaded = map(sem, ("cond_l", "rows_l", "subj_l", "const_l"))
        wtp_loaded, wb_loaded, w3_loaded, w3_asked = map(sem, ("wtp_l", "wb_l", "w3_l", "w3_asked"))
        x_loaded = [sem(f"x_l{i}") for i in range(2)]
        stored = sem("stored")
        warm_set, subj_padded, ones_done, ones_r_done = map(sem, ("warm_set", "subj_padded", "ones_done", "ones_r_done"))
        bd_cleared, cond_rows_done = sem("bd_cleared"), sem("cond_rows_done")
        onehot_done, sel_done, l10_done = sem("onehot_done"), sem("sel_done"), sem("l10_done")
        qt_mm, qt_done, l3raw_done, l3_done = sem("qt_mm"), sem("qt_done"), sem("l3raw_done"), sem("l3_done")
        p_mm, bd_act, bd_dve = sem("p_mm"), sem("bd_act"), sem("bd_dve")
        ql3_done, ql3_hi_done, ql3_lo_done = sem("ql3_done"), sem("ql3_hi_done"), sem("ql3_lo_done")
        c_mm, c_act, c_dve = sem("c_mm"), sem("c_act"), sem("c_dve")
        gt_mm, h_mm, gt_done, h_done, mask_done = map(sem, ("gt_mm", "h_mm", "gt_done", "h_done", "mask_done"))
        m_done, m_hi_done, m_lo_done = sem("m_done"), sem("m_hi_done"), sem("m_lo_done")
        a_mm, x2t_done, x2t_hi_done, x2t_lo_done = map(sem, ("a_mm", "x2t_done", "x2t_hi_done", "x2t_lo_done"))
        h_hi_done, h_lo_done = sem("h_hi_done"), sem("h_lo_done")
        z_mm, z_done, z_hi_done, z_lo_done = map(sem, ("z_mm", "z_done", "z_hi_done", "z_lo_done"))
        y_mm, y_act, y_dve = sem("y_mm"), sem("y_act"), sem("y_dve")

        block = ctx.enter_context(nc.Block())

        @block.sync
        def _(sp):
            sp.dma_start(rows_sb[:, :], idx_row.partition_broadcast(P)).then_inc(rows_loaded, 16)
            sp.dma_start(cond_col[:, :], idx_col).then_inc(cond_loaded, 16)
            sp.dma_start(wtp_sb[:, :], wtp).then_inc(wtp_loaded, 16)
            sp.dma_start(x_sb[:, 0:2], x[:, 0:2]).then_inc(x_loaded[0], 16)
            sp.wait_ge(w3_asked, 1)
            sp.dma_start(x_sb[:, 2:G], x[:, 2:G]).then_inc(x_loaded[1], 16)
            sp.dma_start(m_sb[:, :, :], wb).then_inc(wb_loaded, 16)
            for n in range(G // 2):
                sp.wait_ge(y_act, n + 1)
                sp.wait_ge(y_dve, n + 1)
                sp.dma_start(out[:, 2 * n:2 * n + 2], y[:, 2 * n:2 * n + 2]).then_inc(stored, 16)
            sp.wait_ge(stored, 16 * (G // 2))

        @block.gpsimd
        def _(pool):
            pool.wait_ge(cond_loaded, 16)
            nc.gpsimd.tensor_scalar(cond_rows[:, :], cond_col[:, 0:1], float(R4), cond_col[:, 1:2],
                                    ALU.mult, ALU.add).then_inc(cond_rows_done, 1)
            pool.wait_ge(cond_rows_done, 1)
            pool.indirect_dma_start(w3_rows[:, :], None, w3,
                                    bass.IndirectOffsetOnAxis(ap=cond_rows[:, :], axis=0),
                                    engine_sem=w3_asked).then_inc(w3_loaded, 16)
            pool.wait_ge(h_done, 1)
            pool.wait_ge(h_hi_done, 1)
            nc.gpsimd.tensor_tensor(h_lo[:, :], h[:, :], h_hi[:, :].bitcast(fp32), ALU.subtract).then_inc(h_lo_done, 1)
            pool.wait_ge(wb_loaded, 16)
            pool.wait_ge(const_loaded, 16)
            for k in range(KC):
                diag = m_sb[:, k, k * P:(k + 1) * P]
                nc.gpsimd.tensor_tensor(diag, diag, eye_p, ALU.add).then_inc(m_done, 1)
            pool.wait_ge(m_hi_done, 1)
            nc.gpsimd.tensor_tensor(m_lo[:, :, :], m_sb[:, :, :], m_hi[:, :, :].bitcast(fp32),
                                    ALU.subtract).then_inc(m_lo_done, 1)

        @block.scalar
        def _(act):
            act.dma_start(subj_sb[0:SPAD, :], subj).then_inc(subj_loaded, 16)
            act.dma_start(const_sb[:, :], const).then_inc(const_loaded, 16)
            act.wait_ge(ones_done, 1)
            nc.scalar.copy(ones_r[:, :], ones[:, :]).then_inc(ones_r_done, 1)
            act.wait_ge(h_mm, 1)
            nc.scalar.copy(h[:, :], h_ps).then_inc(h_done, 1)
            nc.scalar.copy(h_hi[:, :], h_ps).then_inc(h_hi_done, 1)
            for n in range(2):
                act.wait_ge(qt_mm, n + 1)
                nc.scalar.copy(qt[:, HALF * n:HALF * (n + 1), :], qt_ps[n]).then_inc(qt_done, 1)
            act.wait_ge(ql3_done, 1)
            nc.scalar.copy(ql3_hi[:, :, :], ql3[:, :, :]).then_inc(ql3_hi_done, 1)
            act.wait_ge(bd_cleared, 1)
            for n in range(2):
                act.wait_ge(p_mm, n + 1)
                for j in range(J // 2, J):
                    q = slice(C * j, C * j + C)
                    last = nc.scalar.copy(bd[q, HALF * n:HALF * (n + 1), q], p_ps[n][q])
                last.then_inc(bd_act, 1)
            act.wait_ge(gt_mm, KC * KC)
            nc.scalar.copy(gt[:, :, :], gt_ps).then_inc(gt_done, 1)
            for j in range(0, J, 2):
                act.wait_ge(c_mm, j + 1)
                nc.scalar.copy(cb[:, :, j, :], c_ps[j].rearrange("p (g d) -> p g d", g=G)).then_inc(c_act, 1)
            act.wait_ge(m_done, KC)
            nc.scalar.copy(m_hi[:, :, :], m_sb[:, :, :]).then_inc(m_hi_done, 1)

            def high_part(n):
                pair = slice(2 * n, 2 * n + 2)
                act.wait_ge(x2t_done, n + 1)
                nc.scalar.copy(x2t_hi[:, pair], x2t[:, pair]).then_inc(x2t_hi_done, 1)

            high_part(0)
            high_part(1)
            high_part(2)
            high_part(3)
            act.wait_ge(z_done, 1)
            nc.scalar.copy(z_hi[:, :], z[:, :]).then_inc(z_hi_done, 1)
            for g in range(0, G, 2):
                act.wait_ge(y_mm, g + 1)
                nc.scalar.copy(y[:, g, :], y_ps[g % len(y_ps)][:, 0:T]).then_inc(y_act, 1)

        @block.vector
        def _(dve):
            nc.vector.memset(warm[:, :], 0.0).then_inc(warm_set, 1)
            nc.vector.memset(subj_sb[SPAD:P, :], 0.0).then_inc(subj_padded, 1)
            nc.vector.memset(ones[:, :], 1.0).then_inc(ones_done, 1)
            nc.vector.memset(bd[:, :, :], 0.0).then_inc(bd_cleared, 1)
            dve.wait_ge(rows_loaded, 16)
            dve.wait_ge(subj_loaded, 16)
            pattern = onehot[0:SROWS, :].rearrange("p (b r) -> p b r", r=R4)
            nc.vector.scalar_tensor_tensor(
                out=pattern, in0=rows_sb[0:SROWS, 0:B].unsqueeze(2).broadcast_to([SROWS, B, R4]),
                scalar=subject_of[0:SROWS, :], in1=pattern, op0=ALU.is_equal, op1=ALU.mult).then_inc(onehot_done, 1)
            dve.wait_ge(const_loaded, 16)
            for n in range(2):
                q = slice(ER * n, ER * n + ER)
                nc.vector.tensor_scalar(mask[q, :], rows_sb[q, B + B // 2 * n:B + B // 2 * (n + 1)],
                                        expert_of[q, :], scale_of[q, :],
                                        ALU.is_equal, ALU.mult).then_inc(mask_done, 1)
            blocks = l10[:, :, :].rearrange("p g (a b) -> p a g b", b=R4)
            for n, part in enumerate((slice(0, C8), slice(C8, SW // C))):
                dve.wait_ge(sel_done, n + 1)
                nc.vector.transpose(blocks[:, part],
                                    sel_ps[n].rearrange("p (a g b) -> p a g b", g=G, b=R4)).then_inc(l10_done, 1)
            dve.wait_ge(w3_loaded, 16)
            nc.vector.transpose(l3raw[:, :, :].rearrange("p g (a b) -> p a g b", b=R4),
                                w3_rows[:, :].rearrange("p (a g b) -> p a g b", g=G, b=R4)).then_inc(l3raw_done, 1)
            dve.wait_ge(l3raw_done, 1)
            nc.vector.tensor_tensor(l3[:, :, :], l3raw[:, :, :], eye_c.unsqueeze(1).broadcast_to([P, G, C]),
                                    ALU.add).then_inc(l3_done, 1)
            dve.wait_ge(l3_done, 1)
            dve.wait_ge(qt_done, 2)
            nc.vector.tensor_tensor(ql3[:, :, :], l3[:, :, :], qt[:, :, C:C + 1].broadcast_to([P, G, C]),
                                    ALU.mult).then_inc(ql3_done, 1)
            dve.wait_ge(bd_cleared, 1)
            for n in range(2):
                dve.wait_ge(p_mm, n + 1)
                for j in range(J // 2):
                    q = slice(C * j, C * j + C)
                    last = nc.vector.tensor_copy(bd[q, HALF * n:HALF * (n + 1), q], p_ps[n][q])
                last.then_inc(bd_dve, 1)
                if n == 0:
                    dve.wait_ge(ql3_hi_done, 1)
                    nc.vector.tensor_tensor(ql3_lo[:, :, :], ql3[:, :, :], ql3_hi[:, :, :].bitcast(fp32),
                                            ALU.subtract).then_inc(ql3_lo_done, 1)
            for j in range(1, J, 2):
                dve.wait_ge(c_mm, j + 1)
                nc.vector.tensor_copy(cb[:, :, j, :], c_ps[j].rearrange("p (g d) -> p g d", g=G)).then_inc(c_dve, 1)
            dve.wait_ge(c_act, J // 2)
            dve.wait_ge(c_dve, J // 2)

            def add_bias(n):
                dve.wait_ge(a_mm, n + 1)
                pair = slice(2 * n, 2 * n + 2)
                bias = cb[:, pair].rearrange("p g j d -> p g (j d)").unsqueeze(2).broadcast_to([P, 2, KC, P])
                nc.vector.tensor_tensor(x2t[:, pair], a_ps[n][:, :].rearrange("p (g k n) -> p g k n", g=2, k=KC),
                                        bias, ALU.add).then_inc(x2t_done, 1)

            def low_part(n):
                dve.wait_ge(x2t_hi_done, n + 1)
                pair = slice(2 * n, 2 * n + 2)
                nc.vector.tensor_tensor(x2t_lo[:, pair], x2t[:, pair], x2t_hi[:, pair].bitcast(fp32),
                                        ALU.subtract).then_inc(x2t_lo_done, 1)

            for n in range(G // 2):
                add_bias(n)
            low_part(0)
            low_part(1)
            dve.wait_ge(z_mm, 1)
            dve.wait_ge(mask_done, 2)
            nc.vector.tensor_tensor(z[:, :].rearrange("p (b d) -> p b d", d=C),
                                    z_ps[:, :].rearrange("p (b d) -> p b d", d=C),
                                    mask[:, :].unsqueeze(2).broadcast_to([P, B // 2, C]), ALU.mult).then_inc(z_done, 1)
            low_part(2)
            dve.wait_ge(z_hi_done, 1)
            nc.vector.tensor_tensor(z_lo[:, :], z[:, :], z_hi[:, :].bitcast(fp32), ALU.subtract).then_inc(z_lo_done, 1)
            low_part(3)
            for g in range(1, G, 2):
                dve.wait_ge(y_mm, g + 1)
                nc.vector.tensor_copy(y[:, g, :], y_ps[g % len(y_ps)][:, 0:T]).then_inc(y_dve, 1)

        @block.tensor
        def _(pe):
            mm = nc.tensor.matmul

            def keep_warm(n):
                for _ in range(n):
                    mm(warm_ps[:, :], warm[:, :], warm[:, 0:1].broadcast_to([P, 512]), start=True, stop=True)

            pe.wait_ge(warm_set, 1)
            keep_warm(WARM[0])
            pe.wait_ge(subj_padded, 1)
            pe.wait_ge(onehot_done, 1)
            mm(sel_ps[0], onehot, table[:, 0:C8 * C], start=True, stop=True).then_inc(sel_done, 1)
            mm(sel_ps[1], onehot, table[:, C8 * C:SW], start=True, stop=True).then_inc(sel_done, 1)
            keep_warm(WARM[1])
            pe.wait_ge(const_loaded, 16)
            pe.wait_ge(wtp_loaded, 16)
            for c in range(KC):
                for n in range(2):
                    last = mm(h_ps[ER * n:ER * n + ER, :], ab_sb[:, c, 1, :], wtp_sb[:, 1, c, :],
                              start=(c == 0), stop=(c == KC - 1), tile_position=(0, ER * n))
            last.then_inc(h_mm, 1)
            pe.wait_ge(l10_done, 2)
            for g in range(G):
                for j in range(J):
                    q = slice(C * j, C * j + C)
                    last = mm(qt_ps[g // HALF][q, g % HALF, :], l10[q, g, 0:C], l10[q, g, C:C + QW],
                              start=True, stop=True, tile_position=(C * j, C * j))
                if g % HALF == HALF - 1:
                    last.then_inc(qt_mm, 1)
            def adapters_in(k):
                for c in range(KC):
                    mm(gt_ps[:, k, :], wtp_sb[:, 0, c, k * P:(k + 1) * P], ab_sb[:, c, 0, :],
                       start=(c == 0), stop=(c == KC - 1)).then_inc(gt_mm, 1)

            keep_warm(WARM[2])
            adapters_in(0)
            pe.wait_ge(l3_done, 1)
            for g in range(G):
                if g % HALF == 0:
                    pe.wait_ge(qt_done, g // HALF + 1)
                for j in range(J):
                    q = slice(C * j, C * j + C)
                    last = mm(p_ps[g // HALF][q, g % HALF, :], qt[q, g, 0:C], l3[q, g, :], start=True, stop=True,
                              tile_position=(C * j, C * j))
                if g % HALF == HALF - 1:
                    last.then_inc(p_mm, 1)

            def left_factors(n):
                if n < 2:
                    pe.wait_ge(x_loaded[n], 16)
                if n % 2 == 0:
                    pe.wait_ge(bd_act, n // 2 + 1)
                    pe.wait_ge(bd_dve, n // 2 + 1)
                for g in range(2 * n, 2 * n + 2):
                    for k in range(KC):
                        at = ((g % 2) * KC + k) * P
                        last = mm(a_ps[n][:, at:at + P], x_sb[:, g, k * P:(k + 1) * P], bd[:, g, :],
                                  start=True, stop=True)
                last.then_inc(a_mm, 1)

            adapters_in(1)
            keep_warm(WARM[3])
            left_factors(0)
            pe.wait_ge(ones_r_done, 1)
            pe.wait_ge(ql3_hi_done, 1)
            pe.wait_ge(ql3_lo_done, 1)
            pe.wait_ge(gt_done, 1)
            for j in range(J):
                q = slice(C * j, C * j + C)
                mm(c_ps[j], ones_r[q, :], ql3_hi[q, :, :], start=True, stop=False, tile_position=(C * j, 0))
                mm(c_ps[j], ones_r[q, :], ql3_lo[q, :, :], start=False, stop=True,
                   tile_position=(C * j, 0)).then_inc(c_mm, 1)
            left_factors(1)
            left_factors(2)
            left_factors(3)
            pe.wait_ge(x2t_done, G // 2)
            for k in range(KC):
                for n in range(2):
                    last = mm(z_ps[ER * n:ER * n + ER, :], gt[:, k, :], x2t[:, HALF * n:HALF * (n + 1), k, :],
                              start=(k == 0), stop=(k == KC - 1), tile_position=(0, ER * n))
            last.then_inc(z_mm, 1)
            pe.wait_ge(m_lo_done, 1)

            def through_base(g):
                if g % 2 == 0:
                    pe.wait_ge(x2t_lo_done, g // 2 + 1)
                if g >= len(y_ps):
                    before = g - len(y_ps)
                    pe.wait_ge(y_dve if before % 2 else y_act, before // 2 + 1)
                for k in range(KC):
                    acc = y_ps[g % len(y_ps)][:, 0:T]
                    mm(acc, x2t_hi[:, g, k, :], m_hi[:, k, :], start=(k == 0), stop=False)
                    mm(acc, x2t_hi[:, g, k, :], m_lo[:, k, :], start=False, stop=False)
                    mm(acc, x2t_lo[:, g, k, :], m_hi[:, k, :], start=False, stop=False)

            def through_adapter(g):
                n = g // HALF
                q = slice(ER * n, ER * n + ER)
                at = g % HALF * P
                acc = y_ps[g % len(y_ps)][:, 0:T]
                mm(acc, z_hi[q, at:at + P], h_hi[q, :], start=False, stop=False, tile_position=(ER * n, 0))
                mm(acc, z_hi[q, at:at + P], h_lo[q, :], start=False, stop=False, tile_position=(ER * n, 0))
                mm(acc, z_lo[q, at:at + P], h_hi[q, :], start=False, stop=True,
                   tile_position=(ER * n, 0)).then_inc(y_mm, 1)

            for g in range(4):
                through_base(g)
            pe.wait_ge(h_hi_done, 1)
            pe.wait_ge(h_lo_done, 1)
            pe.wait_ge(z_hi_done, 1)
            pe.wait_ge(z_lo_done, 1)
            for g in range(4):
                through_adapter(g)
            for g in range(4, G):
                through_base(g)
                through_adapter(g)



def kernel(**inputs):
    import numpy as _np
    import concourse.bacc as _bacc
    from concourse import mybir as _mybir
    from concourse.bass_utils import run_bass_kernel_spmd as _run

    a = {k: _np.asarray(v) for k, v in inputs.items()}
    f32 = a["x"].dtype

    w0 = a["L0_cond_weights"].reshape(SUBJECTS, C8, R4, C).transpose(0, 2, 1, 3).reshape(SROWS, C8 * C)
    w1 = a["L1_cond_weights"].reshape(SUBJECTS, C, C8, R4).transpose(0, 3, 2, 1).reshape(SROWS, C8 * C)
    bias = _np.repeat(a["fside_8xS_0"], R4, axis=0)
    eye = _np.eye(C, dtype=f32).reshape(C8, R4, C).transpose(1, 0, 2).reshape(R4, C8 * C)
    table = _np.concatenate([_np.concatenate([w1, w0, bias], 1),
                             _np.concatenate([eye, eye, _np.zeros((R4, C), f32)], 1)], 0)
    table = _np.concatenate([table, _np.zeros((SPAD - len(table), SW), f32)], 0)
    pattern = _np.tile(_np.eye(R4, dtype=f32), (SPAD // R4, B))
    pattern[SROWS + R4:] = 0
    part = _np.arange(P)
    scale = _np.tile(_np.repeat(a["L2_cond_scaling"], RANK), P // ER)[:, None]
    subject = (part[:SPAD] // R4)[:, None].astype(f32)
    const = _np.concatenate([(part % ER // RANK)[:, None].astype(f32), scale,
                             _np.tile(_np.eye(C, dtype=f32), (J, 1)), _np.eye(P, dtype=f32)], 1)

    def by_partition(m):
        return m.reshape(KC, P, -1).transpose(1, 0, 2)

    ab = _np.stack([by_partition(a["L2_cond_A"].reshape(ER, T).T),
                    by_partition(a["L2_cond_B_w"].transpose(1, 0, 2).reshape(T, ER))], 2)

    def jg(idx):
        return idx.reshape(G, J).T.reshape(B)

    cond = jg(a["itok_B_1_198"])
    arrays = {
        "idx_col": _np.stack([_np.repeat(cond, R4), (part % R4).astype(cond.dtype)], 1),
        "idx_row": _np.concatenate([jg(a["itok_B_0_7"]), a["itok_B_0_3"]]),
        "subj": _np.concatenate([table, pattern, subject], 1),
        "const": _np.concatenate([const, ab.reshape(P, -1)], 1),
        "wtp": _np.stack([by_partition(a["L2_cond_Wt"]), by_partition(a["L2_cond_Wp"].T)], 1),
        "x": a["x"].reshape(G, J, C, T).transpose(1, 2, 0, 3).reshape(P, G, T),
        "wb": by_partition(a["L2_cond_W_base"].T),
        "w3": a["L3_cond_weights"].transpose(0, 2, 1).reshape(CONDITIONS, C8, R4, C)
              .transpose(0, 2, 1, 3).reshape(CONDITIONS * R4, C8 * C),
    }
    arrays = {f"in_{k}": _np.ascontiguousarray(v) for k, v in arrays.items()}
    nc = _bacc.Bacc("TRN2", target_bir_lowering=False, num_devices=1)
    args = [nc.dram_tensor(k, v.shape, _mybir.dt.from_np(v.dtype), kind="ExternalInput").ap()
            for k, v in arrays.items()]
    out = nc.dram_tensor("out_y", (P, G, T), _mybir.dt.from_np(f32), kind="ExternalOutput").ap()
    cond_resid(nc, *args, out)
    r = _run(nc, [arrays], core_ids=[0])
    y = r.results[0]["out_y"]
    return y.reshape(J, C, G, T).transpose(2, 0, 1, 3).reshape(B, C, T)
```

```python
import concourse.bass as bass
from concourse import mybir
from contextlib import ExitStack

B, C, T = 32, 32, 256
SUBJECTS, CONDITIONS = 8, 200
EXPERTS, RANK = 4, 16
P = 128
J = P // C
G = B // J
KC = T // P
ER = EXPERTS * RANK
R4 = P // B
C8 = C // R4
SROWS = SUBJECTS * R4
QW = C + R4
SW = 2 * C8 * C + C
HALF = G // 2
CW = 2 + J // 2 + C + P + KC * 2 * ER
SPAD = 2 * SROWS
WARM = (7, 1)


def cond_resid(nc, idx_col, idx_row, subj, const, wtp, x, wb, w3, out):
    fp32, fp32r, bf16, i32 = mybir.dt.float32, mybir.dt.float32r, mybir.dt.bfloat16, mybir.dt.int32
    ALU = mybir.AluOpType

    with ExitStack() as ctx:
        def sb(name, shape, dt=fp32):
            return ctx.enter_context(nc.sbuf_tensor(name, shape, dt))

        def sem(name):
            return ctx.enter_context(nc.semaphore(name))

        cond_col = sb("cond_col", [P, 2], i32)
        cond_rows = sb("cond_rows", [P, 1], i32)
        rows_sb = sb("rows_sb", [P, 2 * B], i32)
        subj_sb = sb("subj_sb", [P, SW + P + 1])
        const_sb = sb("const_sb", [P, CW])
        wtp_sb = sb("wtp_sb", [P, 2, KC, T])
        x_sb = sb("x_sb", [P, G, T])
        m_sb = sb("m_sb", [P, KC, T])
        table = subj_sb[:, 0:SW]
        onehot = subj_sb[:, SW:SW + P]
        subject_of = subj_sb[:, SW + P:SW + P + 1]
        expert_of, scale_of = const_sb[:, 0:1], const_sb[:, 1:2]
        quad = const_sb[:, 2:2 + J // 2]
        eye_c = const_sb[:, CW - KC * 2 * ER - P - C:CW - KC * 2 * ER - P]
        eye_p = const_sb[:, CW - KC * 2 * ER - P:CW - KC * 2 * ER]
        ab_sb = const_sb[:, CW - KC * 2 * ER:CW].rearrange("p (c w n) -> p c w n", c=KC, w=2)

        w3_rows = sb("w3_rows", [P, C8 * C])
        l3raw = sb("l3raw", [P, G, C])
        l3 = sb("l3", [P, G, C])
        l10 = sb("l10", [P, G, SW // C * R4])
        qt = sb("qt", [P, G, QW])
        bd = sb("bd", [P, G, P])
        ql3 = sb("ql3", [P, G, C])
        ql3_parts = sb("ql3_parts", [P, 2, G, C], fp32r)
        quad_r = sb("quad_r", [P, J // 2], fp32r)
        cb = sb("cb", [P, G, P])
        x2t = sb("x2t", [P, G, KC, P])
        x2t_hi = sb("x2t_hi", [P, G, KC, P], fp32r)
        x2t_lo = sb("x2t_lo", [P, G, KC, P], fp32r)
        m_hi = sb("m_hi", [P, KC, T], fp32r)
        m_lo = sb("m_lo", [P, KC, T], fp32r)
        gt = sb("gt", [P, KC, ER])
        h = sb("h", [P, T])
        h_hi = sb("h_hi", [P, T], fp32r)
        h_lo = sb("h_lo", [P, T], fp32r)
        mask = sb("mask", [P, 2, 2 * J])
        z = sb("z", [ER, 2, 2, 2 * P])
        z_parts = sb("z_parts", [P, 2, 2, 2 * P], fp32r)
        y = sb("y", [P, G, T])
        warm = sb("warm", [P, P], bf16)

        bank = [ctx.enter_context(nc.psum_tensor(f"bank{i}", [P, 512], fp32)) for i in range(8)]
        sel_ps = [bank[0][:, 0:C8 * C], bank[1][:, 0:SW - C8 * C]]
        qt_ps = [bank[n][:, 320:320 + HALF * QW].rearrange("p (g c) -> p g c", g=HALF) for n in (1, 2)]
        p_ps = [bank[i][:, 0:2 * C].rearrange("p (g d) -> p g d", g=2) for i in (3, 0, 1, 2)]
        a_ps = [bank[i] for i in (6, 7, 0, 3)]
        c_ps = [bank[i][:, :].rearrange("p (j g d) -> p j g d", j=J // 2, g=G) for i in (5, 1)]
        gt_ps = bank[4][:, 0:KC * ER].rearrange("p (k n) -> p k n", k=KC)
        h_ps = bank[5][:, 0:T]
        z_ps = [bank[i] for i in (1, 5)]
        y_ps = [bank[i] for i in (2, 6, 7, 4, 0, 3)]
        warm_ps = bank[7]

        cond_loaded, rows_loaded, subj_loaded, const_loaded = map(sem, ("cond_l", "rows_l", "subj_l", "const_l"))
        wp_loaded, wt_loaded, wb_loaded, w3_loaded, w3_asked = map(sem, ("wp_l", "wt_l", "wb_l", "w3_l", "w3_asked"))
        x_loaded = [sem(f"x_l{i}") for i in range(2)]
        stored = sem("stored")
        warm_set, subj_padded, quad_r_done = map(sem, ("warm_set", "subj_padded", "quad_r_done"))
        bd_cleared, cond_rows_done = sem("bd_cleared"), sem("cond_rows_done")
        onehot_done, sel_done, l10_done = sem("onehot_done"), sem("sel_done"), sem("l10_done")
        qt_mm, qt_done, l3raw_done, l3_done = sem("qt_mm"), sem("qt_done"), sem("l3raw_done"), sem("l3_done")
        p_mm, bd_act, bd_dve = sem("p_mm"), sem("bd_act"), sem("bd_dve")
        ql3_done, ql3_hi_done, ql3_lo_done = sem("ql3_done"), sem("ql3_hi_done"), sem("ql3_lo_done")
        c_mm, c_done = sem("c_mm"), sem("c_done")
        gt_mm, h_mm, gt_done, h_done, mask_done = map(sem, ("gt_mm", "h_mm", "gt_done", "h_done", "mask_done"))
        m_done, m_hi_done, m_lo_done = sem("m_done"), sem("m_hi_done"), sem("m_lo_done")
        a_mm, x2t_done, x2t_hi_done, x2t_lo_done = map(sem, ("a_mm", "x2t_done", "x2t_hi_done", "x2t_lo_done"))
        h_hi_done, h_lo_done = sem("h_hi_done"), sem("h_lo_done")
        z_mm, z_done, z_hi_done, z_lo_done = map(sem, ("z_mm", "z_done", "z_hi_done", "z_lo_done"))
        y_mm, y_act, y_dve = sem("y_mm"), sem("y_act"), sem("y_dve")

        block = ctx.enter_context(nc.Block())

        @block.sync
        def _(sp):
            sp.dma_start(subj_sb[0:SPAD, :], subj).then_inc(subj_loaded, 16)
            sp.dma_start(cond_col[:, :], idx_col).then_inc(cond_loaded, 16)
            sp.dma_start(wtp_sb[:, 1], wtp[:, 1]).then_inc(wp_loaded, 16)
            sp.dma_start(wtp_sb[:, 0], wtp[:, 0]).then_inc(wt_loaded, 16)
            sp.dma_start(x_sb[:, 0:2], x[:, 0:2]).then_inc(x_loaded[0], 16)
            sp.wait_ge(w3_asked, 1)
            sp.dma_start(x_sb[:, 2:G], x[:, 2:G]).then_inc(x_loaded[1], 16)
            sp.dma_start(m_sb[:, :, :], wb).then_inc(wb_loaded, 16)
            for n in range(G // 2 - 1):
                sp.wait_ge(y_dve, n + 1)
                sp.wait_ge(y_act, n + 1)
                sp.dma_start(out[:, 2 * n:2 * n + 2], y[:, 2 * n:2 * n + 2]).then_inc(stored, 16)
            sp.wait_ge(y_dve, G // 2)
            sp.dma_start(out[:, G - 2], y[:, G - 2]).then_inc(stored, 16)
            sp.wait_ge(y_act, G // 2)
            sp.dma_start(out[:, G - 1], y[:, G - 1]).then_inc(stored, 16)
            sp.wait_ge(stored, 16 * (G // 2 + 1))

        @block.gpsimd
        def _(pool):
            pool.wait_ge(cond_loaded, 16)
            nc.gpsimd.tensor_scalar(cond_rows[:, :], cond_col[:, 0:1], float(R4), cond_col[:, 1:2],
                                    ALU.mult, ALU.add).then_inc(cond_rows_done, 1)
            pool.wait_ge(cond_rows_done, 1)
            pool.indirect_dma_start(w3_rows[:, :], None, w3,
                                    bass.IndirectOffsetOnAxis(ap=cond_rows[:, :], axis=0),
                                    engine_sem=w3_asked).then_inc(w3_loaded, 16)
            pool.wait_ge(wb_loaded, 16)
            pool.wait_ge(const_loaded, 16)
            for k in range(KC):
                diag = m_sb[:, k, k * P:(k + 1) * P]
                nc.gpsimd.tensor_tensor(diag, diag, eye_p, ALU.add).then_inc(m_done, 1)
            pool.wait_ge(m_hi_done, 1)
            nc.gpsimd.tensor_tensor(m_lo[:, :, :], m_sb[:, :, :], m_hi[:, :, :].bitcast(fp32),
                                    ALU.subtract).then_inc(m_lo_done, 1)
            pool.wait_ge(h_done, 1)
            pool.wait_ge(h_hi_done, 1)
            nc.gpsimd.tensor_tensor(h_lo[:, :], h[:, :], h_hi[:, :].bitcast(fp32), ALU.subtract).then_inc(h_lo_done, 1)

        @block.scalar
        def _(act):
            act.dma_start(rows_sb[:, :], idx_row.partition_broadcast(P)).then_inc(rows_loaded, 16)
            act.dma_start(const_sb[:, :], const).then_inc(const_loaded, 16)
            act.wait_ge(const_loaded, 16)
            nc.scalar.copy(quad_r[:, :], quad).then_inc(quad_r_done, 1)
            for n in range(2):
                act.wait_ge(qt_mm, n + 1)
                nc.scalar.copy(qt[:, HALF * n:HALF * (n + 1), :], qt_ps[n]).then_inc(qt_done, 1)
            act.wait_ge(h_mm, 2 * KC)
            nc.scalar.copy(h[:, :], h_ps).then_inc(h_done, 1)
            act.wait_ge(ql3_done, 1)
            for n in range(2):
                q = slice(P // 2 * n, P // 2 * (n + 1))
                nc.scalar.copy(ql3_parts[q, n], ql3[q]).then_inc(ql3_hi_done, 1)
            act.wait_ge(gt_mm, KC * KC)
            nc.scalar.copy(gt[:, :, :], gt_ps).then_inc(gt_done, 1)
            act.wait_ge(bd_cleared, 1)
            for n in range(G // 2):
                act.wait_ge(p_mm, n + 1)
                for j in range(J // 2, J):
                    q = slice(C * j, C * j + C)
                    last = nc.scalar.copy(bd[q, 2 * n:2 * n + 2, q], p_ps[n][q])
                last.then_inc(bd_act, 1)
            nc.scalar.copy(h_hi[:, :], h_ps).then_inc(h_hi_done, 1)
            act.wait_ge(m_done, KC)
            nc.scalar.copy(m_hi[:, :, :], m_sb[:, :, :]).then_inc(m_hi_done, 1)
            for n in range(2):
                tiles = slice(HALF * n, HALF * (n + 1))
                for i in range(2):
                    act.wait_ge(c_mm, J // 2 * (i + 1))
                    last = nc.scalar.copy(
                        cb[:, tiles, C * J // 2 * i:C * J // 2 * (i + 1)].rearrange("p g (j d) -> p g j d", j=J // 2),
                        c_ps[i][:, :, tiles].rearrange("p j g d -> p g j d"))
                last.then_inc(c_done, 1)

            def high_part(n):
                pair = slice(2 * n, 2 * n + 2)
                act.wait_ge(x2t_done, n + 1)
                nc.scalar.copy(x2t_hi[:, pair], x2t[:, pair]).then_inc(x2t_hi_done, 1)

            def adapter_high_part(n):
                act.wait_ge(z_done, n + 1)
                nc.scalar.copy(z_parts[0:ER, n], z[:, n]).then_inc(z_hi_done, 1)

            def result(g):
                act.wait_ge(y_mm, g + 1)
                nc.scalar.copy(y[:, g, :], y_ps[g % len(y_ps)][:, 0:T]).then_inc(y_act, 1)

            high_part(0)
            high_part(1)
            high_part(2)
            high_part(3)
            adapter_high_part(0)
            adapter_high_part(1)
            result(1)
            for g in range(3, G, 2):
                result(g)

        @block.vector
        def _(dve):
            nc.vector.memset(warm[:, :], 0.0).then_inc(warm_set, 1)
            nc.vector.memset(subj_sb[SPAD:P, :], 0.0).then_inc(subj_padded, 1)
            nc.vector.memset(bd[:, :, :], 0.0).then_inc(bd_cleared, 1)
            dve.wait_ge(rows_loaded, 16)
            dve.wait_ge(subj_loaded, 16)
            pattern = onehot[0:SROWS, :].rearrange("p (b r) -> p b r", r=R4)
            nc.vector.scalar_tensor_tensor(
                out=pattern, in0=rows_sb[0:SROWS, 0:B].unsqueeze(2).broadcast_to([SROWS, B, R4]),
                scalar=subject_of[0:SROWS, :], in1=pattern, op0=ALU.is_equal, op1=ALU.mult).then_inc(onehot_done, 1)
            dve.wait_ge(const_loaded, 16)
            adapters = rows_sb[:, B:2 * B].rearrange("r (n p b) -> r n p b", n=2, p=2)
            for p in range(2):
                q = slice(ER * p, ER * p + ER)
                nc.vector.tensor_scalar(mask[q], adapters[q, :, p], expert_of[q, :], scale_of[q, :],
                                        ALU.is_equal, ALU.mult).then_inc(mask_done, 1)
            blocks = l10[:, :, :].rearrange("p g (a b) -> p a g b", b=R4)
            for n, part in enumerate((slice(0, C8), slice(C8, SW // C))):
                dve.wait_ge(sel_done, n + 1)
                nc.vector.transpose(blocks[:, part],
                                    sel_ps[n].rearrange("p (a g b) -> p a g b", g=G, b=R4)).then_inc(l10_done, 1)
            dve.wait_ge(w3_loaded, 16)
            nc.vector.transpose(l3raw[:, :, :].rearrange("p g (a b) -> p a g b", b=R4),
                                w3_rows[:, :].rearrange("p (a g b) -> p a g b", g=G, b=R4)).then_inc(l3raw_done, 1)
            dve.wait_ge(l3raw_done, 1)
            nc.vector.tensor_tensor(l3[:, :, :], l3raw[:, :, :], eye_c.unsqueeze(1).broadcast_to([P, G, C]),
                                    ALU.add).then_inc(l3_done, 1)
            dve.wait_ge(l3_done, 1)
            dve.wait_ge(qt_done, 2)
            nc.vector.tensor_tensor(ql3[:, :, :], l3[:, :, :], qt[:, :, C:C + 1].broadcast_to([P, G, C]),
                                    ALU.mult).then_inc(ql3_done, 1)

            def bias_low_part(n):
                q, other = slice(P // 2 * n, P // 2 * (n + 1)), slice(P // 2 * (1 - n), P // 2 * (2 - n))
                dve.wait_ge(ql3_hi_done, n + 1)
                nc.vector.tensor_tensor(ql3_parts[other, n], ql3[q], ql3_parts[q, n].bitcast(fp32),
                                        ALU.subtract).then_inc(ql3_lo_done, 1)

            bias_low_part(0)
            dve.wait_ge(bd_cleared, 1)
            for n in range(G // 2):
                dve.wait_ge(p_mm, n + 1)
                for j in range(J // 2):
                    q = slice(C * j, C * j + C)
                    last = nc.vector.tensor_copy(bd[q, 2 * n:2 * n + 2, q], p_ps[n][q])
                last.then_inc(bd_dve, 1)
                if n == 1:
                    bias_low_part(1)

            def add_bias(n):
                dve.wait_ge(a_mm, n + 1)
                dve.wait_ge(c_done, n // 2 + 1)
                pair = slice(2 * n, 2 * n + 2)
                bias = cb[:, pair].unsqueeze(2).broadcast_to([P, 2, KC, P])
                nc.vector.tensor_tensor(x2t[:, pair], a_ps[n][:, :].rearrange("p (g k n) -> p g k n", g=2, k=KC),
                                        bias, ALU.add).then_inc(x2t_done, 1)

            def low_part(n):
                dve.wait_ge(x2t_hi_done, n + 1)
                pair = slice(2 * n, 2 * n + 2)
                nc.vector.tensor_tensor(x2t_lo[:, pair], x2t[:, pair], x2t_hi[:, pair].bitcast(fp32),
                                        ALU.subtract).then_inc(x2t_lo_done, 1)

            def mask_adapters(n):
                dve.wait_ge(z_mm, n + 1)
                dve.wait_ge(mask_done, 2)
                for p in range(2):
                    q = slice(ER * p, ER * p + ER)
                    last = nc.vector.tensor_tensor(
                        z[:, n, p].rearrange("r (b d) -> r b d", d=C),
                        z_ps[n][q, 0:2 * P].rearrange("r (b d) -> r b d", d=C),
                        mask[q, n].unsqueeze(2).broadcast_to([ER, 2 * J, C]), ALU.mult)
                last.then_inc(z_done, 1)

            def adapter_low_part(n):
                dve.wait_ge(z_hi_done, n + 1)
                nc.vector.tensor_tensor(z_parts[ER:P, n], z[:, n], z_parts[0:ER, n].bitcast(fp32),
                                        ALU.subtract).then_inc(z_lo_done, 1)

            def result(g):
                dve.wait_ge(y_mm, g + 1)
                nc.vector.tensor_copy(y[:, g, :], y_ps[g % len(y_ps)][:, 0:T]).then_inc(y_dve, 1)

            add_bias(0)
            add_bias(1)
            low_part(0)
            add_bias(2)
            add_bias(3)
            mask_adapters(0)
            low_part(1)
            adapter_low_part(0)
            mask_adapters(1)
            low_part(2)
            result(0)
            adapter_low_part(1)
            low_part(3)
            for g in range(2, G, 2):
                result(g)

        @block.tensor
        def _(pe):
            mm = nc.tensor.matmul

            def keep_warm(n):
                for _ in range(n):
                    mm(warm_ps[:, :], warm[:, :], warm[:, 0:1].broadcast_to([P, 512]), start=True, stop=True)

            def adapters_out(c):
                for n in range(2):
                    mm(h_ps[ER * n:ER * n + ER, :], ab_sb[:, c, 1, :], wtp_sb[:, 1, c, :], start=(c == 0),
                       stop=(c == KC - 1), tile_position=(0, ER * n)).then_inc(h_mm, 1)

            def adapters_in(k):
                for c in range(KC):
                    mm(gt_ps[:, k, :], wtp_sb[:, 0, c, k * P:(k + 1) * P], ab_sb[:, c, 0, :],
                       start=(c == 0), stop=(c == KC - 1)).then_inc(gt_mm, 1)

            def left_factors(n):
                if n < 2:
                    pe.wait_ge(x_loaded[n], 16)
                pe.wait_ge(bd_act, n + 1)
                pe.wait_ge(bd_dve, n + 1)
                for g in range(2 * n, 2 * n + 2):
                    for k in range(KC):
                        at = ((g % 2) * KC + k) * P
                        last = mm(a_ps[n][:, at:at + P], x_sb[:, g, k * P:(k + 1) * P], bd[:, g, :],
                                  start=True, stop=True)
                last.then_inc(a_mm, 1)

            def adapter_products(n):
                for k in range(KC):
                    for p in range(2):
                        first = HALF * n + 2 * p
                        last = mm(z_ps[n][ER * p:ER * p + ER, 0:2 * P], gt[:, k, :], x2t[:, first:first + 2, k, :],
                                  start=(k == 0), stop=(k == KC - 1), tile_position=(0, ER * p))
                last.then_inc(z_mm, 1)

            def through_base(g):
                if g % 2 == 0:
                    pe.wait_ge(x2t_lo_done, g // 2 + 1)
                if g >= len(y_ps):
                    before = g - len(y_ps)
                    pe.wait_ge(y_act if before % 2 else y_dve, before // 2 + 1)
                for k in range(KC):
                    acc = y_ps[g % len(y_ps)][:, 0:T]
                    mm(acc, x2t_hi[:, g, k, :], m_hi[:, k, :], start=(k == 0), stop=False)
                    mm(acc, x2t_hi[:, g, k, :], m_lo[:, k, :], start=False, stop=False)
                    mm(acc, x2t_lo[:, g, k, :], m_hi[:, k, :], start=False, stop=False)

            def through_adapter(g):
                n, p, at = g // HALF, g // 2 % 2, g % 2 * P
                if g % HALF == 0:
                    pe.wait_ge(z_hi_done, n + 1)
                    pe.wait_ge(z_lo_done, n + 1)
                acc = y_ps[g % len(y_ps)][:, 0:T]
                mm(acc, z_parts[:, n, p, at:at + P], h_lo[:, :], start=False, stop=False)
                mm(acc, z_parts[:, n, p, at:at + P], h_hi[:, :], start=False, stop=True).then_inc(y_mm, 1)

            pe.wait_ge(warm_set, 1)
            keep_warm(WARM[0])
            pe.wait_ge(subj_padded, 1)
            pe.wait_ge(onehot_done, 1)
            mm(sel_ps[0], onehot, table[:, 0:C8 * C], start=True, stop=True).then_inc(sel_done, 1)
            mm(sel_ps[1], onehot, table[:, C8 * C:SW], start=True, stop=True).then_inc(sel_done, 1)
            pe.wait_ge(const_loaded, 16)
            pe.wait_ge(wp_loaded, 16)
            adapters_out(0)
            pe.wait_ge(l10_done, 2)
            for g in range(G):
                for j in range(J):
                    q = slice(C * j, C * j + C)
                    last = mm(qt_ps[g // HALF][q, g % HALF, :], l10[q, g, 0:C], l10[q, g, C:C + QW],
                              start=True, stop=True, tile_position=(C * j, C * j))
                if g % HALF == HALF - 1:
                    last.then_inc(qt_mm, 1)
            adapters_out(1)
            keep_warm(WARM[1])
            pe.wait_ge(wt_loaded, 16)
            adapters_in(0)
            adapters_in(1)
            pe.wait_ge(l3_done, 1)
            for g in range(G):
                if g % HALF == 0:
                    pe.wait_ge(qt_done, g // HALF + 1)
                for j in range(J):
                    q = slice(C * j, C * j + C)
                    last = mm(p_ps[g // 2][q, g % 2, :], qt[q, g, 0:C], l3[q, g, :], start=True, stop=True,
                              tile_position=(C * j, C * j))
                if g % 2 == 1:
                    last.then_inc(p_mm, 1)

            left_factors(0)
            pe.wait_ge(h_hi_done, 1)
            pe.wait_ge(bd_act, 3)
            pe.wait_ge(bd_dve, 3)
            pe.wait_ge(quad_r_done, 1)
            for j in range(J):
                pe.wait_ge(ql3_hi_done, j // 2 + 1)
                pe.wait_ge(ql3_lo_done, j // 2 + 1)
                mm(c_ps[j // 2][:, j % 2], quad_r[:, j % 2:j % 2 + 1].broadcast_to([P, P]), ql3_parts[:, j // 2],
                   start=True, stop=True).then_inc(c_mm, 1)
            left_factors(1)
            left_factors(2)
            left_factors(3)
            pe.wait_ge(c_done, 2)
            pe.wait_ge(gt_done, 1)
            pe.wait_ge(x2t_done, 2)
            adapter_products(0)
            pe.wait_ge(m_lo_done, 1)

            through_base(0)
            through_base(1)
            pe.wait_ge(x2t_done, 4)
            adapter_products(1)
            pe.wait_ge(h_lo_done, 1)
            through_base(2)
            for g in range(3):
                through_adapter(g)
            for g in range(3, G):
                through_base(g)
                through_adapter(g)



def kernel(**inputs):
    import numpy as _np
    import concourse.bacc as _bacc
    from concourse import mybir as _mybir
    from concourse.bass_utils import run_bass_kernel_spmd as _run

    a = {k: _np.asarray(v) for k, v in inputs.items()}
    f32 = a["x"].dtype

    w0 = a["L0_cond_weights"].reshape(SUBJECTS, C8, R4, C).transpose(0, 2, 1, 3).reshape(SROWS, C8 * C)
    w1 = a["L1_cond_weights"].reshape(SUBJECTS, C, C8, R4).transpose(0, 3, 2, 1).reshape(SROWS, C8 * C)
    bias = _np.repeat(a["fside_8xS_0"], R4, axis=0)
    eye = _np.eye(C, dtype=f32).reshape(C8, R4, C).transpose(1, 0, 2).reshape(R4, C8 * C)
    table = _np.concatenate([_np.concatenate([w1, w0, bias], 1),
                             _np.concatenate([eye, eye, _np.zeros((R4, C), f32)], 1)], 0)
    table = _np.concatenate([table, _np.zeros((SPAD - len(table), SW), f32)], 0)
    pattern = _np.tile(_np.eye(R4, dtype=f32), (SPAD // R4, B))
    pattern[SROWS + R4:] = 0
    part = _np.arange(P)
    scale = _np.tile(_np.repeat(a["L2_cond_scaling"], RANK), P // ER)[:, None]
    subject = (part[:SPAD] // R4)[:, None].astype(f32)
    const = _np.concatenate([(part % ER // RANK)[:, None].astype(f32), scale,
                             _np.tile(_np.repeat(_np.eye(J // 2, dtype=f32), C, axis=0), (2, 1)),
                             _np.tile(_np.eye(C, dtype=f32), (J, 1)), _np.eye(P, dtype=f32)], 1)

    def by_partition(m):
        return m.reshape(KC, P, -1).transpose(1, 0, 2)

    ab = _np.stack([by_partition(a["L2_cond_A"].reshape(ER, T).T),
                    by_partition(a["L2_cond_B_w"].transpose(1, 0, 2).reshape(T, ER))], 2)

    def jg(idx):
        return idx.reshape(G, J).T.reshape(B)

    cond = jg(a["itok_B_1_198"])
    arrays = {
        "idx_col": _np.stack([_np.repeat(cond, R4), (part % R4).astype(cond.dtype)], 1),
        "idx_row": _np.concatenate([jg(a["itok_B_0_7"]), a["itok_B_0_3"]]),
        "subj": _np.concatenate([table, pattern, subject], 1),
        "const": _np.concatenate([const, ab.reshape(P, -1)], 1),
        "wtp": _np.stack([by_partition(a["L2_cond_Wt"]), by_partition(a["L2_cond_Wp"].T)], 1),
        "x": a["x"].reshape(G, J, C, T).transpose(1, 2, 0, 3).reshape(P, G, T),
        "wb": by_partition(a["L2_cond_W_base"].T),
        "w3": a["L3_cond_weights"].transpose(0, 2, 1).reshape(CONDITIONS, C8, R4, C)
              .transpose(0, 2, 1, 3).reshape(CONDITIONS * R4, C8 * C),
    }
    arrays = {f"in_{k}": _np.ascontiguousarray(v) for k, v in arrays.items()}
    nc = _bacc.Bacc("TRN2", target_bir_lowering=False, num_devices=1)
    args = [nc.dram_tensor(k, v.shape, _mybir.dt.from_np(v.dtype), kind="ExternalInput").ap()
            for k, v in arrays.items()]
    out = nc.dram_tensor("out_y", (P, G, T), _mybir.dt.from_np(f32), kind="ExternalOutput").ap()
    cond_resid(nc, *args, out)
    r = _run(nc, [arrays], core_ids=[0])
    y = r.results[0]["out_y"]
    return y.reshape(J, C, G, T).transpose(2, 0, 1, 3).reshape(B, C, T)
```
